# Optimizing a Trainium2 kernel written in Bass

```python
import numpy as np
import jax
import jax.numpy as jnp

def _softmax(x, axis=-1):
    return jax.nn.softmax(x, axis=axis)

def _gelu(x):
    return jax.nn.gelu(x, approximate=True)

def _silu(x):
    return jax.nn.silu(x)

def _sigmoid(x):
    return jax.nn.sigmoid(x)

def _layernorm(x, axis=-1, eps=1e-05):
    m = jnp.mean(x, axis=axis, keepdims=True)
    v = jnp.var(x, axis=axis, keepdims=True)
    return (x - m) / jnp.sqrt(v + eps)

def _scatter_add(tgt, idx, src, axis=0):
    return tgt.at[idx].add(src)

def _segment_sum(src, seg, n):
    return jax.ops.segment_sum(src, seg, n)
kernel_name = 'mk_adj_resnorm_d1_adj_r2_853fbe'

def setup_inputs(seed: int=0):
    np.random.seed(seed)
    _w = jnp.asarray

    def _rec_inputs():
        import jax
        import jax.numpy as jnp
        _gk = jax.random.key(seed)
        x = -0.000929 + 1 * jax.random.normal(jax.random.fold_in(_gk, 1), (8192, 64), jnp.float32)
        _a = jax.random.bernoulli(jax.random.fold_in(_gk, 2), 0.00195312, (8192, 8192))
        _a = jnp.logical_or(_a, jnp.swapaxes(_a, -1, -2))
        _a = jnp.logical_or(_a, jnp.eye(8192, dtype=bool))
        _af = _a.astype(jnp.float32)
        _af = _af * jax.random.uniform(jax.random.fold_in(_gk, 3), (8192, 8192), jnp.float32, 0.05, 1)
        adj = _af
        return (x, adj)
    x, adj = _rec_inputs()

    def _L0_gnn_setup():
        import jax, jax.numpy as jnp
        import numpy as np
        P_DROP = 0.1
        key = jax.random.key(seed)
        k1, k2, k3 = jax.random.split(key, 3)
        N, D = (8192, 64)
        x = jax.random.normal(k1, (N, D), dtype=jnp.float32)
        adj = jax.random.uniform(k2, (N, N), dtype=jnp.float32)
        u = jax.random.uniform(k3, (N, D), dtype=jnp.float32)
        return {'x': x, 'adj': adj, 'u': u}
    _L0_gnn_all = _L0_gnn_setup()
    _L0_gnn_in = {k: v for k, v in _L0_gnn_all.items() if k in ('u',)}
    del _L0_gnn_all
    return {'x': x, 'adj': adj, 'L0_gnn_u': _L0_gnn_in['u']}

def reference(x, adj, L0_gnn_u):
    import jax
    import jax.numpy as jnp

    def _L0_gnn_ref(x, adj, u):
        import jax, jax.numpy as jnp
        import numpy as np
        P_DROP = 0.1
        keep = (u >= P_DROP).astype(x.dtype)
        x_drop = x * keep / (1.0 - P_DROP)
        return jnp.matmul(adj, x_drop)
    x = _layernorm(x + _L0_gnn_ref(x, adj, L0_gnn_u), axis=-1)
    return x

_drawn_inputs = setup_inputs


def setup_inputs(seed=0):
    import zlib

    import numpy as np

    out = dict(_drawn_inputs(seed))
    spreads = {}
    factors = {}
    for name, (base, spread) in spreads.items():
        noise = np.random.default_rng([zlib.crc32(name.encode()), seed]).standard_normal(out[name].shape)
        drawn = base * np.exp(spread * noise) if base else spread * noise
        out[name] = jnp.asarray(drawn.astype(out[name].dtype))
    for name, factor in factors.items():
        out[name] = (out[name] * factor).astype(out[name].dtype)
    return out
```

```python
from contextlib import ExitStack

import concourse.bass as bass
from concourse import mybir

P = 128
N = 8192
D = 64
CHUNKS = N // P
BLOCK = 1024
BLOCKS = N // BLOCK
CHUNKS_PER_BLOCK = BLOCK // P
BANK = 512
HALVES = BLOCK // BANK
K_PER_TILE = 4
TILE = K_PER_TILE * BLOCK
TILES = CHUNKS // K_PER_TILE
SLOTS = 4
SPLITS = 2
GROUPS = TILES // SLOTS
DMA = 16

P_DROP = 0.1
EPS = 1e-5


def dropout_matmul_layernorm(nc, x, u, adj, out):
    fp32 = mybir.dt.float32
    fp32r = mybir.dt.float32r
    ALU = mybir.AluOpType
    ACT = mybir.ActivationFunctionType
    AX = mybir.AxisListType

    x_dram = x.rearrange("(p c) d -> p (c d)", p=P)
    u_dram = u.rearrange("(p c) d -> p (c d)", p=P)
    out_dram = out.rearrange("(p c) d -> p (c d)", p=P)
    out_cols = CHUNKS_PER_BLOCK * D

    with ExitStack() as ctx:
        def sbuf(name, shape, dt=fp32):
            return ctx.enter_context(nc.sbuf_tensor(name, shape, dt))

        def psum(name, shape):
            return ctx.enter_context(nc.psum_tensor(name, shape, fp32))

        def semaphore(name):
            return ctx.enter_context(nc.semaphore(name))

        x_sb = sbuf("x_sb", [P, CHUNKS, D])
        dropped = sbuf("dropped", [P, CHUNKS, D])
        weights = sbuf("weights", [P, CHUNKS, 2 * D], fp32r)
        raw = sbuf("raw", [P, SLOTS, TILE])
        high = sbuf("high", [P, SPLITS, TILE], fp32r)
        low = sbuf("low", [P, SPLITS, TILE], fp32r)
        join = sbuf("join", [P, D])
        sums = sbuf("sums", [P, BLOCK])
        rows = sbuf("rows", [P, CHUNKS_PER_BLOCK, D])
        stats = sbuf("stats", [P, CHUNKS_PER_BLOCK, 6])
        mean = sbuf("mean", [P, CHUNKS_PER_BLOCK])
        apart = sbuf("apart", [P, CHUNKS_PER_BLOCK])
        squares = sbuf("squares", [P, CHUNKS_PER_BLOCK])
        between = sbuf("between", [P, CHUNKS_PER_BLOCK])
        var_eps = sbuf("var_eps", [P, CHUNKS_PER_BLOCK])
        std = sbuf("std", [P, CHUNKS_PER_BLOCK])
        rstd = sbuf("rstd", [P, CHUNKS_PER_BLOCK])
        centred = sbuf("centred", [P, CHUNKS_PER_BLOCK, D])
        normed = sbuf("normed", [P, CHUNKS_PER_BLOCK, D])

        acc = psum("acc", [P, BLOCK])
        turned = psum("turned", [P, CHUNKS_PER_BLOCK, D])

        x_loaded = semaphore("x_loaded")
        u_loaded = semaphore("u_loaded")
        raw_loaded = [semaphore(f"raw_loaded{s}") for s in range(SLOTS)]
        drop_scaled = semaphore("drop_scaled")
        x_dropped = semaphore("x_dropped")
        weights_high = semaphore("weights_high")
        weights_ready = semaphore("weights_ready")
        join_zeroed = semaphore("join_zeroed")
        join_half = semaphore("join_half")
        join_ready = semaphore("join_ready")
        high_ready = semaphore("high_ready")
        low_ready = semaphore("low_ready")
        tile_multiplied = semaphore("tile_multiplied")
        sums_ready = semaphore("sums_ready")
        block_turned = semaphore("block_turned")
        rows_ready = semaphore("rows_ready")
        stats_ready = semaphore("stats_ready")
        halves_joined = semaphore("halves_joined")
        moments_ready = semaphore("moments_ready")
        var_ready = semaphore("var_ready")
        std_ready = semaphore("std_ready")
        rstd_ready = semaphore("rstd_ready")
        centred_ready = semaphore("centred_ready")
        normed_ready = semaphore("normed_ready")
        out_stored = semaphore("out_stored")

        block = ctx.enter_context(nc.Block())

        @block.sync
        def _(sp):
            sp.dma_start(dropped[:, :, :], u_dram).then_inc(u_loaded, DMA)
            sp.dma_start(x_sb[:, :, :], x_dram).then_inc(x_loaded, DMA)
            for s in range(SLOTS):
                sp.dma_start(raw[:, s, :], adj[s]).then_inc(raw_loaded[s], DMA)
            with sp.Fori(1, BLOCKS * GROUPS) as g:
                for s in range(SLOTS):
                    sp.wait_ge(low_ready, (g - 1) * SLOTS + s + 1)
                    sp.dma_start(raw[:, s, :], adj[g * SLOTS + s]).then_inc(raw_loaded[s], DMA)

        @block.gpsimd
        def _(pool):
            nc.gpsimd.memset(join[:, :], 0.0).then_inc(join_zeroed, 1)
            pool.wait_ge(join_zeroed, 1)
            nc.gpsimd.affine_select(out=join[:, :], in_=join[:, :], compare_op=ALU.not_equal, fill=1.0,
                                    base=0, pattern=[[-1, D]], channel_multiplier=1).then_inc(join_half, 1)
            pool.wait_ge(join_half, 1)
            nc.gpsimd.affine_select(out=join[:, :], in_=join[:, :], compare_op=ALU.not_equal, fill=1.0,
                                    base=-D, pattern=[[-1, D]], channel_multiplier=1).then_inc(join_ready, 1)

            def finish(b, first):
                pool.wait_ge(moments_ready, b + 1)
                nc.gpsimd.tensor_tensor(
                    centred[:, :, :], rows[:, :, :],
                    mean[:, :].unsqueeze(2).broadcast_to([P, CHUNKS_PER_BLOCK, D]),
                    ALU.subtract).then_inc(centred_ready, 1)
                pool.wait_ge(centred_ready, b + 1)
                pool.wait_ge(rstd_ready, b + 1)
                if not first:
                    pool.wait_ge(out_stored, b * DMA)
                nc.gpsimd.tensor_tensor(
                    normed[:, :, :], centred[:, :, :],
                    rstd[:, :].unsqueeze(2).broadcast_to([P, CHUNKS_PER_BLOCK, D]),
                    ALU.mult).then_inc(normed_ready, 1)
                pool.wait_ge(normed_ready, b + 1)
                pool.dma_start(out_dram[:, bass.ds(b * out_cols, out_cols)],
                               normed[:, :, :]).then_inc(out_stored, DMA)

            finish(0, True)
            with pool.Fori(1, BLOCKS) as b:
                finish(b, False)
            pool.wait_ge(out_stored, BLOCKS * DMA)

        @block.scalar
        def _(act):
            act.wait_ge(x_dropped, 1)
            nc.scalar.copy(weights[:, :, 0:D], dropped[:, :, :]).then_inc(weights_high, 1)

            def split_high(b, g, s, after_multiply=True):
                t = b * TILES + g * SLOTS + s
                act.wait_ge(raw_loaded[s], (b * GROUPS + g + 1) * DMA)
                if after_multiply:
                    act.wait_ge(tile_multiplied, t - SPLITS + 1)
                nc.scalar.copy(high[:, s % SPLITS, :], raw[:, s, :]).then_inc(high_ready, 1)

            def take_sums(b, first=False):
                act.wait_ge(tile_multiplied, (b + 1) * TILES)
                nc.scalar.copy(sums[:, :], acc[:, :]).then_inc(sums_ready, 1)

            def deviation(b):
                act.wait_ge(var_ready, b + 1)
                nc.scalar.activation(std[:, :], var_eps[:, :], ACT.Sqrt).then_inc(std_ready, 1)

            for s in range(SLOTS):
                split_high(0, 0, s, s >= SPLITS)
            with act.Fori(0, BLOCKS - 1) as b:
                with act.Fori(1, GROUPS) as g:
                    for s in range(SLOTS):
                        split_high(b, g, s)
                split_high(b + 1, 0, 0)
                take_sums(b)
                for s in range(1, SLOTS):
                    split_high(b + 1, 0, s)
                deviation(b)
            with act.Fori(1, GROUPS) as g:
                for s in range(SLOTS):
                    split_high(BLOCKS - 1, g, s)
            take_sums(BLOCKS - 1)
            deviation(BLOCKS - 1)

        @block.vector
        def _(dve):
            dve.wait_ge(u_loaded, DMA)
            nc.vector.tensor_scalar(dropped[:, :, :], dropped[:, :, :], P_DROP, 1.0 / (1.0 - P_DROP),
                                    ALU.is_ge, ALU.mult).then_inc(drop_scaled, 1)
            dve.wait_ge(drop_scaled, 1)
            dve.wait_ge(x_loaded, DMA)
            nc.vector.tensor_tensor(dropped[:, :, :], dropped[:, :, :], x_sb[:, :, :],
                                    ALU.mult).then_inc(x_dropped, 1)
            dve.wait_ge(weights_high, 1)
            nc.vector.tensor_tensor(weights[:, :, D:2 * D], dropped[:, :, :],
                                    weights[:, :, 0:D].bitcast(fp32),
                                    ALU.subtract).then_inc(weights_ready, 1)

            def split_low(b, g, s):
                t = b * TILES + g * SLOTS + s
                dve.wait_ge(high_ready, t + 1)
                nc.vector.tensor_tensor(low[:, s % SPLITS, :], raw[:, s, :],
                                        high[:, s % SPLITS, :].bitcast(fp32),
                                        ALU.subtract).then_inc(low_ready, 1)

            def statistics(b, first):
                dve.wait_ge(block_turned, b + 1)
                if first is False:
                    dve.wait_ge(normed_ready, b)
                nc.vector.tensor_tensor(
                    rows[:, :, :], turned[:, :, :],
                    x_sb[:, bass.ds(b * CHUNKS_PER_BLOCK, CHUNKS_PER_BLOCK), :],
                    ALU.add).then_inc(rows_ready, 1)
                dve.wait_ge(rows_ready, b + 1)
                for c in range(CHUNKS_PER_BLOCK):
                    last = nc.vector.bn_stats(stats[:, c, :], rows[:, c, :])
                last.then_inc(stats_ready, 1)
                dve.wait_ge(stats_ready, b + 1)
                nc.vector.tensor_tensor(mean[:, :], stats[:, :, 1], stats[:, :, 4], ALU.add)
                nc.vector.tensor_tensor(apart[:, :], stats[:, :, 1], stats[:, :, 4],
                                        ALU.subtract)
                nc.vector.tensor_tensor(squares[:, :], stats[:, :, 2], stats[:, :, 5],
                                        ALU.add).then_inc(halves_joined, 1)
                dve.wait_ge(halves_joined, b + 1)
                nc.vector.scalar_tensor_tensor(between[:, :], apart[:, :], 0.25, apart[:, :],
                                               ALU.mult, ALU.mult)
                nc.vector.tensor_scalar(squares[:, :], squares[:, :], 1.0 / D, EPS,
                                        ALU.mult, ALU.add)
                nc.vector.tensor_scalar(mean[:, :], mean[:, :], 0.5, None,
                                        ALU.mult).then_inc(moments_ready, 1)
                dve.wait_ge(moments_ready, b + 1)
                nc.vector.tensor_tensor(var_eps[:, :], squares[:, :], between[:, :],
                                        ALU.add).then_inc(var_ready, 1)

            def reciprocal(b):
                dve.wait_ge(std_ready, b + 1)
                nc.vector.reciprocal(rstd[:, :], std[:, :]).then_inc(rstd_ready, 1)

            for s in range(SLOTS):
                split_low(0, 0, s)

            def middle_block(b, first):
                with dve.Fori(1, GROUPS) as g:
                    for s in range(SLOTS):
                        split_low(b, g, s)
                for s in range(SLOTS - 1):
                    split_low(b + 1, 0, s)
                statistics(b, first)
                split_low(b + 1, 0, SLOTS - 1)
                reciprocal(b)

            middle_block(0, True)
            with dve.Fori(1, BLOCKS - 1) as b:
                middle_block(b, False)
            with dve.Fori(1, GROUPS) as g:
                for s in range(SLOTS):
                    split_low(BLOCKS - 1, g, s)
            statistics(BLOCKS - 1, False)
            reciprocal(BLOCKS - 1)

        @block.tensor
        def _(pe):
            def multiply(b, t):
                pe.wait_ge(low_ready, b * TILES + t + 1)
                for j in range(K_PER_TILE):
                    k = t * K_PER_TILE + j
                    for part in (high, low):
                        for h in range(HALVES):
                            cols = slice(h * BANK, (h + 1) * BANK)
                            src = slice(j * BLOCK + h * BANK, j * BLOCK + (h + 1) * BANK)
                            last = nc.tensor.matmul(
                                acc[:, cols], weights[:, k, :], part[:, t % SPLITS, src],
                                start=(k == 0 and part is high),
                                stop=(k == CHUNKS - 1 and part is low))
                last.then_inc(tile_multiplied, 1)

            def turn(b):
                for c in range(CHUNKS_PER_BLOCK):
                    last = nc.tensor.matmul(turned[:, c, :], sums[:, c * P:(c + 1) * P], join[:, :],
                                            start=True, stop=True)
                last.then_inc(block_turned, 1)

            pe.wait_ge(weights_ready, 1)
            multiply(0, 0)

            def middle_block(b):
                for t in range(1, TILES):
                    multiply(b, t)
                pe.wait_ge(sums_ready, b + 1)
                multiply(b + 1, 0)
                turn(b)

            pe.wait_ge(join_ready, 1)
            with pe.Fori(0, BLOCKS - 1) as b:
                middle_block(b)
            for t in range(1, TILES):
                multiply(BLOCKS - 1, t)
            pe.wait_ge(sums_ready, BLOCKS)
            turn(BLOCKS - 1)


def kernel(x, adj, L0_gnn_u):
    import numpy as np
    import concourse.bacc as bacc
    from concourse.bass_utils import run_bass_kernel_spmd

    tiles = np.asarray(adj).reshape(P, BLOCKS, CHUNKS_PER_BLOCK, P, TILES, K_PER_TILE)
    tiles = tiles.transpose(1, 4, 3, 5, 2, 0).reshape(BLOCKS * TILES, P, TILE)
    arrays = {
        "x_dram": np.ascontiguousarray(x),
        "u_dram": np.ascontiguousarray(L0_gnn_u),
        "adj_dram": np.ascontiguousarray(tiles),
    }
    nc = bacc.Bacc("TRN2", target_bir_lowering=False, num_devices=1)
    fp32 = mybir.dt.float32
    args = [nc.dram_tensor(name, a.shape, fp32, kind="ExternalInput").ap() for name, a in arrays.items()]
    out = nc.dram_tensor("out_dram", (N, D), fp32, kind="ExternalOutput").ap()
    dropout_matmul_layernorm(nc, *args, out)
    got = run_bass_kernel_spmd(nc, [arrays], core_ids=[0])
    return got.results[0]["out_dram"]
```

```python
from contextlib import ExitStack

import concourse.bass as bass
from concourse import mybir

P = 128
N = 8192
D = 64
CHUNKS = N // P
BLOCK = 1024
BLOCKS = N // BLOCK
CHUNKS_PER_BLOCK = BLOCK // P
BANK = 512
HALVES = BLOCK // BANK
K_PER_TILE = 4
TILE = K_PER_TILE * BLOCK
TILES = CHUNKS // K_PER_TILE
SLOTS = 4
K_PER_PIECE = 2
PIECES = K_PER_TILE // K_PER_PIECE
PIECE = K_PER_PIECE * BLOCK
SPLITS = 4
LAST = BLOCKS * TILES - 1
GROUPS = TILES // SLOTS
DMA = 16

P_DROP = 0.1
EPS = 1e-5


def dropout_matmul_layernorm(nc, x, u, adj, out):
    fp32 = mybir.dt.float32
    fp32r = mybir.dt.float32r
    ALU = mybir.AluOpType
    ACT = mybir.ActivationFunctionType
    AX = mybir.AxisListType

    x_dram = x.rearrange("(p c) d -> p (c d)", p=P)
    u_dram = u.rearrange("(p c) d -> p (c d)", p=P)
    out_dram = out.rearrange("(p c) d -> p (c d)", p=P)
    out_cols = CHUNKS_PER_BLOCK * D

    with ExitStack() as ctx:
        def sbuf(name, shape, dt=fp32):
            return ctx.enter_context(nc.sbuf_tensor(name, shape, dt))

        def psum(name, shape):
            return ctx.enter_context(nc.psum_tensor(name, shape, fp32))

        def semaphore(name):
            return ctx.enter_context(nc.semaphore(name))

        x_sb = sbuf("x_sb", [P, CHUNKS, D])
        dropped = sbuf("dropped", [P, CHUNKS, D])
        weights = sbuf("weights", [P, CHUNKS, 2 * D], fp32r)
        raw = sbuf("raw", [P, SLOTS, TILE])
        high = sbuf("high", [P, SPLITS, PIECE], fp32r)
        low = sbuf("low", [P, SPLITS, PIECE], fp32r)
        join = sbuf("join", [P, D])
        sums = sbuf("sums", [P, BLOCK])
        rows = sbuf("rows", [P, CHUNKS_PER_BLOCK, D])
        stats = sbuf("stats", [P, CHUNKS_PER_BLOCK, 6])
        mean = sbuf("mean", [P, CHUNKS_PER_BLOCK])
        apart = sbuf("apart", [P, CHUNKS_PER_BLOCK])
        squares = sbuf("squares", [P, CHUNKS_PER_BLOCK])
        between = sbuf("between", [P, CHUNKS_PER_BLOCK])
        var_eps = sbuf("var_eps", [P, CHUNKS_PER_BLOCK])
        std = sbuf("std", [P, CHUNKS_PER_BLOCK])
        rstd = sbuf("rstd", [P, CHUNKS_PER_BLOCK])
        centred = sbuf("centred", [P, CHUNKS_PER_BLOCK, D])
        normed = sbuf("normed", [P, CHUNKS_PER_BLOCK, D])

        acc = psum("acc", [P, BLOCK])
        turned = psum("turned", [P, CHUNKS_PER_BLOCK, D])

        x_loaded = semaphore("x_loaded")
        u_loaded = semaphore("u_loaded")
        raw_loaded = [semaphore(f"raw_loaded{s}") for s in range(SLOTS)]
        last_loaded = [semaphore(f"last_loaded{j}") for j in range(K_PER_TILE)]
        drop_scaled = semaphore("drop_scaled")
        x_dropped = semaphore("x_dropped")
        weights_high = semaphore("weights_high")
        weights_ready = semaphore("weights_ready")
        join_zeroed = semaphore("join_zeroed")
        join_half = semaphore("join_half")
        join_ready = semaphore("join_ready")
        high_ready = semaphore("high_ready")
        low_ready = semaphore("low_ready")
        multiplied = semaphore("multiplied")
        sums_ready = semaphore("sums_ready")
        block_turned = semaphore("block_turned")
        rows_ready = semaphore("rows_ready")
        stats_ready = semaphore("stats_ready")
        halves_joined = semaphore("halves_joined")
        moments_ready = semaphore("moments_ready")
        var_ready = semaphore("var_ready")
        std_ready = semaphore("std_ready")
        rstd_ready = semaphore("rstd_ready")
        centred_ready = semaphore("centred_ready")
        normed_ready = semaphore("normed_ready")
        out_stored = semaphore("out_stored")

        block = ctx.enter_context(nc.Block())

        def last_place(j):
            buffer = (LAST * PIECES + j // K_PER_PIECE) % SPLITS
            start = j % K_PER_PIECE * BLOCK
            return buffer, slice(start, start + BLOCK)

        @block.sync
        def _(sp):
            sp.dma_start(dropped[:, :, :], u_dram).then_inc(u_loaded, DMA)
            sp.dma_start(x_sb[:, :, :], x_dram).then_inc(x_loaded, DMA)
            for s in range(SLOTS):
                sp.dma_start(raw[:, s, :], adj[s]).then_inc(raw_loaded[s], DMA)

            def load(g, s):
                sp.wait_ge(low_ready, ((g - 1) * SLOTS + s + 1) * PIECES)
                sp.dma_start(raw[:, s, :], adj[g * SLOTS + s]).then_inc(raw_loaded[s], DMA)

            with sp.Fori(1, BLOCKS * GROUPS - 1) as g:
                for s in range(SLOTS):
                    load(g, s)
            for s in range(SLOTS - 1):
                load(BLOCKS * GROUPS - 1, s)
            sp.wait_ge(low_ready, (LAST - SLOTS + 1) * PIECES)
            for j in range(K_PER_TILE):
                chunk = slice(j * BLOCK, (j + 1) * BLOCK)
                sp.dma_start(raw[:, SLOTS - 1, chunk], adj[LAST][:, chunk]).then_inc(last_loaded[j], DMA)

        @block.gpsimd
        def _(pool):
            nc.gpsimd.memset(join[:, :], 0.0).then_inc(join_zeroed, 1)
            pool.wait_ge(join_zeroed, 1)
            nc.gpsimd.affine_select(out=join[:, :], in_=join[:, :], compare_op=ALU.not_equal, fill=1.0,
                                    base=0, pattern=[[-1, D]], channel_multiplier=1).then_inc(join_half, 1)
            pool.wait_ge(join_half, 1)
            nc.gpsimd.affine_select(out=join[:, :], in_=join[:, :], compare_op=ALU.not_equal, fill=1.0,
                                    base=-D, pattern=[[-1, D]], channel_multiplier=1).then_inc(join_ready, 1)

            def finish(b, first):
                pool.wait_ge(moments_ready, b + 1)
                nc.gpsimd.tensor_tensor(
                    centred[:, :, :], rows[:, :, :],
                    mean[:, :].unsqueeze(2).broadcast_to([P, CHUNKS_PER_BLOCK, D]),
                    ALU.subtract).then_inc(centred_ready, 1)
                pool.wait_ge(centred_ready, b + 1)
                pool.wait_ge(rstd_ready, b + 1)
                if not first:
                    pool.wait_ge(out_stored, b * DMA)
                nc.gpsimd.tensor_tensor(
                    normed[:, :, :], centred[:, :, :],
                    rstd[:, :].unsqueeze(2).broadcast_to([P, CHUNKS_PER_BLOCK, D]),
                    ALU.mult).then_inc(normed_ready, 1)
                pool.wait_ge(normed_ready, b + 1)
                pool.dma_start(out_dram[:, bass.ds(b * out_cols, out_cols)],
                               normed[:, :, :]).then_inc(out_stored, DMA)

            finish(0, True)
            with pool.Fori(1, BLOCKS) as b:
                finish(b, False)
            pool.wait_ge(out_stored, BLOCKS * DMA)

        @block.scalar
        def _(act):
            act.wait_ge(x_dropped, 1)
            nc.scalar.copy(weights[:, :, 0:D], dropped[:, :, :]).then_inc(weights_high, 1)

            def split_high(b, g, s, first=False):
                act.wait_ge(raw_loaded[s], (b * GROUPS + g + 1) * DMA)
                for i in range(PIECES):
                    q = s * PIECES + i
                    if not (first and q < SPLITS):
                        act.wait_ge(multiplied, (b * TILES + g * SLOTS) * PIECES + q - SPLITS + 1)
                    nc.scalar.copy(high[:, q % SPLITS, :],
                                   raw[:, s, i * PIECE:(i + 1) * PIECE]).then_inc(high_ready, 1)

            def split_last_high():
                for j in range(K_PER_TILE):
                    buffer, chunk = last_place(j)
                    act.wait_ge(last_loaded[j], DMA)
                    act.wait_ge(multiplied, LAST * PIECES + j // K_PER_PIECE - SPLITS + 1)
                    nc.scalar.copy(high[:, buffer, chunk],
                                   raw[:, SLOTS - 1, j * BLOCK:(j + 1) * BLOCK]).then_inc(high_ready, 1)

            def take_sums(b, count):
                act.wait_ge(multiplied, count)
                nc.scalar.copy(sums[:, :], acc[:, :]).then_inc(sums_ready, 1)

            def deviation(b):
                act.wait_ge(var_ready, b + 1)
                nc.scalar.activation(std[:, :], var_eps[:, :], ACT.Sqrt).then_inc(std_ready, 1)

            for s in range(SLOTS):
                split_high(0, 0, s, True)
            with act.Fori(0, BLOCKS - 1) as b:
                with act.Fori(1, GROUPS) as g:
                    for s in range(SLOTS):
                        split_high(b, g, s)
                split_high(b + 1, 0, 0)
                take_sums(b, (b + 1) * TILES * PIECES)
                for s in range(1, SLOTS):
                    split_high(b + 1, 0, s)
                deviation(b)
            with act.Fori(1, GROUPS - 1) as g:
                for s in range(SLOTS):
                    split_high(BLOCKS - 1, g, s)
            for s in range(SLOTS - 1):
                split_high(BLOCKS - 1, GROUPS - 1, s)
            split_last_high()
            take_sums(BLOCKS - 1, LAST * PIECES + K_PER_TILE)
            deviation(BLOCKS - 1)

        @block.vector
        def _(dve):
            dve.wait_ge(u_loaded, DMA)
            nc.vector.tensor_scalar(dropped[:, :, :], dropped[:, :, :], P_DROP, 1.0 / (1.0 - P_DROP),
                                    ALU.is_ge, ALU.mult).then_inc(drop_scaled, 1)
            dve.wait_ge(drop_scaled, 1)
            dve.wait_ge(x_loaded, DMA)
            nc.vector.tensor_tensor(dropped[:, :, :], dropped[:, :, :], x_sb[:, :, :],
                                    ALU.mult).then_inc(x_dropped, 1)
            dve.wait_ge(weights_high, 1)
            nc.vector.tensor_tensor(weights[:, :, D:2 * D], dropped[:, :, :],
                                    weights[:, :, 0:D].bitcast(fp32),
                                    ALU.subtract).then_inc(weights_ready, 1)

            def split_low(b, g, s):
                for i in range(PIECES):
                    q = s * PIECES + i
                    dve.wait_ge(high_ready, (b * TILES + g * SLOTS) * PIECES + q + 1)
                    nc.vector.tensor_tensor(low[:, q % SPLITS, :], raw[:, s, i * PIECE:(i + 1) * PIECE],
                                            high[:, q % SPLITS, :].bitcast(fp32),
                                            ALU.subtract).then_inc(low_ready, 1)

            def split_last_low():
                for j in range(K_PER_TILE):
                    buffer, chunk = last_place(j)
                    dve.wait_ge(high_ready, LAST * PIECES + j + 1)
                    nc.vector.tensor_tensor(low[:, buffer, chunk],
                                            raw[:, SLOTS - 1, j * BLOCK:(j + 1) * BLOCK],
                                            high[:, buffer, chunk].bitcast(fp32),
                                            ALU.subtract).then_inc(low_ready, 1)

            def statistics(b, first):
                dve.wait_ge(block_turned, b + 1)
                if first is False:
                    dve.wait_ge(normed_ready, b)
                nc.vector.tensor_tensor(
                    rows[:, :, :], turned[:, :, :],
                    x_sb[:, bass.ds(b * CHUNKS_PER_BLOCK, CHUNKS_PER_BLOCK), :],
                    ALU.add).then_inc(rows_ready, 1)
                dve.wait_ge(rows_ready, b + 1)
                for c in range(CHUNKS_PER_BLOCK):
                    last = nc.vector.bn_stats(stats[:, c, :], rows[:, c, :])
                last.then_inc(stats_ready, 1)
                dve.wait_ge(stats_ready, b + 1)
                nc.vector.tensor_tensor(mean[:, :], stats[:, :, 1], stats[:, :, 4], ALU.add)
                nc.vector.tensor_tensor(apart[:, :], stats[:, :, 1], stats[:, :, 4],
                                        ALU.subtract)
                nc.vector.tensor_tensor(squares[:, :], stats[:, :, 2], stats[:, :, 5],
                                        ALU.add).then_inc(halves_joined, 1)
                dve.wait_ge(halves_joined, b + 1)
                nc.vector.scalar_tensor_tensor(between[:, :], apart[:, :], 0.25, apart[:, :],
                                               ALU.mult, ALU.mult)
                nc.vector.tensor_scalar(squares[:, :], squares[:, :], 1.0 / D, EPS,
                                        ALU.mult, ALU.add)
                nc.vector.tensor_scalar(mean[:, :], mean[:, :], 0.5, None,
                                        ALU.mult).then_inc(moments_ready, 1)
                dve.wait_ge(moments_ready, b + 1)
                nc.vector.tensor_tensor(var_eps[:, :], squares[:, :], between[:, :],
                                        ALU.add).then_inc(var_ready, 1)

            def reciprocal(b):
                dve.wait_ge(std_ready, b + 1)
                nc.vector.reciprocal(rstd[:, :], std[:, :]).then_inc(rstd_ready, 1)

            for s in range(SLOTS):
                split_low(0, 0, s)

            def middle_block(b, first):
                with dve.Fori(1, GROUPS) as g:
                    for s in range(SLOTS):
                        split_low(b, g, s)
                for s in range(SLOTS - 1):
                    split_low(b + 1, 0, s)
                statistics(b, first)
                split_low(b + 1, 0, SLOTS - 1)
                reciprocal(b)

            middle_block(0, True)
            with dve.Fori(1, BLOCKS - 1) as b:
                middle_block(b, False)
            with dve.Fori(1, GROUPS - 1) as g:
                for s in range(SLOTS):
                    split_low(BLOCKS - 1, g, s)
            for s in range(SLOTS - 1):
                split_low(BLOCKS - 1, GROUPS - 1, s)
            split_last_low()
            statistics(BLOCKS - 1, False)
            reciprocal(BLOCKS - 1)

        @block.tensor
        def _(pe):
            def multiply_chunk(k, buffer, start):
                for part in (high, low):
                    for h in range(HALVES):
                        last = nc.tensor.matmul(
                            acc[:, h * BANK:(h + 1) * BANK], weights[:, k, :],
                            part[:, buffer, start + h * BANK:start + (h + 1) * BANK],
                            start=(k == 0 and part is high), stop=(k == CHUNKS - 1 and part is low))
                return last

            def multiply(b, t):
                for i in range(PIECES):
                    q = t * PIECES + i
                    pe.wait_ge(low_ready, b * TILES * PIECES + q + 1)
                    for j in range(K_PER_PIECE):
                        last = multiply_chunk(q * K_PER_PIECE + j, q % SPLITS, j * BLOCK)
                    last.then_inc(multiplied, 1)

            def multiply_last():
                for j in range(K_PER_TILE):
                    buffer, chunk = last_place(j)
                    pe.wait_ge(low_ready, LAST * PIECES + j + 1)
                    multiply_chunk(CHUNKS - K_PER_TILE + j, buffer, chunk.start).then_inc(multiplied, 1)

            def turn(b):
                for c in range(CHUNKS_PER_BLOCK):
                    last = nc.tensor.matmul(turned[:, c, :], sums[:, c * P:(c + 1) * P], join[:, :],
                                            start=True, stop=True)
                last.then_inc(block_turned, 1)

            pe.wait_ge(weights_ready, 1)
            multiply(0, 0)

            def middle_block(b):
                for t in range(1, TILES):
                    multiply(b, t)
                pe.wait_ge(sums_ready, b + 1)
                multiply(b + 1, 0)
                turn(b)

            pe.wait_ge(join_ready, 1)
            with pe.Fori(0, BLOCKS - 1) as b:
                middle_block(b)
            for t in range(1, TILES - 1):
                multiply(BLOCKS - 1, t)
            multiply_last()
            pe.wait_ge(sums_ready, BLOCKS)
            turn(BLOCKS - 1)


def kernel(x, adj, L0_gnn_u):
    import numpy as np
    import concourse.bacc as bacc
    from concourse.bass_utils import run_bass_kernel_spmd

    tiles = np.asarray(adj).reshape(P, BLOCKS, CHUNKS_PER_BLOCK, P, TILES, K_PER_TILE)
    tiles = tiles.transpose(1, 4, 3, 5, 2, 0).reshape(BLOCKS * TILES, P, TILE)
    arrays = {
        "x_dram": np.ascontiguousarray(x),
        "u_dram": np.ascontiguousarray(L0_gnn_u),
        "adj_dram": np.ascontiguousarray(tiles),
    }
    nc = bacc.Bacc("TRN2", target_bir_lowering=False, num_devices=1)
    fp32 = mybir.dt.float32
    args = [nc.dram_tensor(name, a.shape, fp32, kind="ExternalInput").ap() for name, a in arrays.items()]
    out = nc.dram_tensor("out_dram", (N, D), fp32, kind="ExternalOutput").ap()
    dropout_matmul_layernorm(nc, *args, out)
    got = run_bass_kernel_spmd(nc, [arrays], core_ids=[0])
    return got.results[0]["out_dram"]
```

```python
from contextlib import ExitStack

import concourse.bass as bass
from concourse import mybir

P = 128
N = 8192
D = 64
CHUNKS = N // P
BANK = 512
HALVES = 2
BLOCK = HALVES * BANK
BLOCKS = N // BLOCK
CHUNKS_PER_BLOCK = BLOCK // P
CHUNKS_PER_HALF = CHUNKS_PER_BLOCK // HALVES
K_PER_PIECE = 2
K_PER_HALF_PIECE = 4
PIECE = K_PER_PIECE * BLOCK
PIECES = CHUNKS // K_PER_PIECE
LAST = BLOCKS * PIECES
SLOTS = 8
SPLITS = 4
GROUPS = PIECES // SLOTS
FINE_PIECES = 4
PARTS = 4
PART = PIECE // PARTS
DMA = 16

P_DROP = 0.1
EPS = 1e-5


def dropout_matmul_layernorm(nc, x, u, adj, out):
    fp32 = mybir.dt.float32
    fp32r = mybir.dt.float32r
    ALU = mybir.AluOpType

    x_dram = x.rearrange("(p c) d -> p (c d)", p=P)
    u_dram = u.rearrange("(p c) d -> p (c d)", p=P)
    out_dram = out.rearrange("(p c) d -> p (c d)", p=P)

    with ExitStack() as ctx:
        def sbuf(name, shape, dt=fp32):
            return ctx.enter_context(nc.sbuf_tensor(name, shape, dt))

        def psum(name, shape):
            return ctx.enter_context(nc.psum_tensor(name, shape, fp32))

        def semaphore(name):
            return ctx.enter_context(nc.semaphore(name))

        x_sb = sbuf("x_sb", [P, CHUNKS, D])
        dropped = sbuf("dropped", [P, CHUNKS, D])
        weights = sbuf("weights", [P, CHUNKS, 2 * D], fp32r)
        raw = sbuf("raw", [P, SLOTS, PIECE])
        high = sbuf("high", [P, SPLITS, PIECE], fp32r)
        low = sbuf("low", [P, SPLITS, PIECE], fp32r)
        join = sbuf("join", [P, D])
        sums = sbuf("sums", [P, BLOCK])
        rows = sbuf("rows", [P, CHUNKS_PER_BLOCK, D])
        stats = sbuf("stats", [P, CHUNKS_PER_BLOCK, 6])
        mean = sbuf("mean", [P, CHUNKS_PER_BLOCK])
        apart = sbuf("apart", [P, CHUNKS_PER_BLOCK])
        squares = sbuf("squares", [P, CHUNKS_PER_BLOCK])
        between = sbuf("between", [P, CHUNKS_PER_BLOCK])
        var_eps = sbuf("var_eps", [P, CHUNKS_PER_BLOCK])
        minus_half = sbuf("minus_half", [P, CHUNKS_PER_BLOCK])
        rstd = sbuf("rstd", [P, CHUNKS_PER_BLOCK])
        centred = sbuf("centred", [P, CHUNKS_PER_BLOCK, D])
        normed = sbuf("normed", [P, CHUNKS_PER_BLOCK, D])

        acc = psum("acc", [P, BLOCK])
        turned = psum("turned", [P, CHUNKS_PER_BLOCK, D])

        x_loaded = semaphore("x_loaded")
        u_loaded = semaphore("u_loaded")
        raw_loaded = [semaphore(f"raw_loaded{s}") for s in range(SLOTS)]
        part_loaded = [semaphore(f"part_loaded{f}") for f in range(FINE_PIECES * PARTS)]
        drop_scaled = semaphore("drop_scaled")
        x_dropped = semaphore("x_dropped")
        weights_high = semaphore("weights_high")
        weights_ready = semaphore("weights_ready")
        minus_half_ready = semaphore("minus_half_ready")
        join_zeroed = semaphore("join_zeroed")
        join_half = semaphore("join_half")
        join_ready = semaphore("join_ready")
        high_ready = semaphore("high_ready")
        low_ready = semaphore("low_ready")
        multiplied = semaphore("multiplied")
        sums_ready = semaphore("sums_ready")
        unit_turned = semaphore("unit_turned")
        rows_ready = semaphore("rows_ready")
        stats_ready = semaphore("stats_ready")
        parities_joined = semaphore("parities_joined")
        moments_ready = semaphore("moments_ready")
        var_ready = semaphore("var_ready")
        rstd_ready = semaphore("rstd_ready")
        centred_ready = semaphore("centred_ready")
        normed_ready = semaphore("normed_ready")
        out_stored = semaphore("out_stored")
        last_centred = semaphore("last_centred")
        last_normed = semaphore("last_normed")
        last_stored = semaphore("last_stored")

        block = ctx.enter_context(nc.Block())

        whole = slice(0, CHUNKS_PER_BLOCK)
        half = [slice(h * CHUNKS_PER_HALF, (h + 1) * CHUNKS_PER_HALF) for h in range(HALVES)]
        FIRST_FINE = LAST - FINE_PIECES
        parts = [(FIRST_FINE + f // PARTS, slice(f % PARTS * PART, (f % PARTS + 1) * PART))
                 for f in range(FINE_PIECES * PARTS)]

        def spread(values, c):
            return values[:, c].unsqueeze(2).broadcast_to([P, c.stop - c.start, D])

        @block.sync
        def _(sp):
            sp.dma_start(dropped[:, :, :], u_dram).then_inc(u_loaded, DMA)
            sp.dma_start(x_sb[:, :, :], x_dram).then_inc(x_loaded, DMA)
            for s in range(SLOTS):
                sp.dma_start(raw[:, s, :], adj[s]).then_inc(raw_loaded[s], DMA)

            def load(g, s):
                sp.wait_ge(low_ready, (g - 1) * SLOTS + s + 1)
                sp.dma_start(raw[:, s, :], adj[g * SLOTS + s]).then_inc(raw_loaded[s], DMA)

            with sp.Fori(1, BLOCKS * GROUPS - 1) as g:
                for s in range(SLOTS):
                    load(g, s)
            for s in range(SLOTS - FINE_PIECES):
                load(BLOCKS * GROUPS - 1, s)
            for f, (piece, part) in enumerate(parts):
                sp.wait_ge(low_ready, piece - SLOTS + 1)
                sp.dma_start(raw[:, piece % SLOTS, part], adj[piece][:, part]).then_inc(part_loaded[f], DMA)

            sp.wait_ge(last_normed, 1)
            start = (CHUNKS - CHUNKS_PER_HALF) * D
            sp.dma_start(out_dram[:, start:], normed[:, half[1], :]).then_inc(last_stored, DMA)
            sp.wait_ge(last_stored, DMA)

        @block.gpsimd
        def _(pool):
            nc.gpsimd.memset(minus_half[:, :], -0.5).then_inc(minus_half_ready, 1)
            nc.gpsimd.memset(join[:, :], 0.0).then_inc(join_zeroed, 1)
            pool.wait_ge(join_zeroed, 1)
            nc.gpsimd.affine_select(out=join[:, :], in_=join[:, :], compare_op=ALU.not_equal, fill=1.0,
                                    base=0, pattern=[[-1, D]], channel_multiplier=1).then_inc(join_half, 1)
            pool.wait_ge(join_half, 1)
            nc.gpsimd.affine_select(out=join[:, :], in_=join[:, :], compare_op=ALU.not_equal, fill=1.0,
                                    base=-D, pattern=[[-1, D]], channel_multiplier=1).then_inc(join_ready, 1)

            pool.wait_ge(minus_half_ready, 1)

            def scale(n, c):
                pool.wait_ge(var_ready, n + 1)
                nc.gpsimd.tensor_tensor(rstd[:, c], var_eps[:, c], minus_half[:, c],
                                        ALU.pow).then_inc(rstd_ready, 1)

            def finish(n, c, first=False):
                pool.wait_ge(moments_ready, n + 1)
                nc.gpsimd.tensor_tensor(centred[:, c, :], rows[:, c, :], spread(mean, c),
                                        ALU.subtract).then_inc(centred_ready, 1)
                scale(n, c)
                pool.wait_ge(centred_ready, n + 1)
                pool.wait_ge(rstd_ready, n + 1)
                if not first:
                    pool.wait_ge(out_stored, n * DMA)
                nc.gpsimd.tensor_tensor(normed[:, c, :], centred[:, c, :], spread(rstd, c),
                                        ALU.mult).then_inc(normed_ready, 1)
                pool.wait_ge(normed_ready, n + 1)
                width = (c.stop - c.start) * D
                pool.dma_start(out_dram[:, bass.ds(n * CHUNKS_PER_BLOCK * D, width)],
                               normed[:, c, :]).then_inc(out_stored, DMA)

            finish(0, whole, True)
            with pool.Fori(1, BLOCKS - 1) as b:
                finish(b, whole)
            finish(BLOCKS - 1, half[0])
            scale(BLOCKS, half[1])
            pool.wait_ge(out_stored, BLOCKS * DMA)

        @block.scalar
        def _(act):
            act.wait_ge(x_dropped, 1)
            nc.scalar.copy(weights[:, :, 0:D], dropped[:, :, :]).then_inc(weights_high, 1)

            def split_high(g, s, buffer_used=True):
                act.wait_ge(raw_loaded[s], (g + 1) * DMA)
                if buffer_used:
                    act.wait_ge(multiplied, g * SLOTS + s - SPLITS + 1)
                nc.scalar.copy(high[:, s % SPLITS, :], raw[:, s, :]).then_inc(high_ready, 1)

            def split_high_parts():
                for f, (piece, part) in enumerate(parts):
                    act.wait_ge(part_loaded[f], DMA)
                    act.wait_ge(multiplied, piece - SPLITS + 1)
                    nc.scalar.copy(high[:, piece % SPLITS, part],
                                   raw[:, piece % SLOTS, part]).then_inc(high_ready, 1)

            def take_sums(done, columns):
                act.wait_ge(multiplied, done)
                nc.scalar.copy(sums[:, columns], acc[:, columns]).then_inc(sums_ready, 1)

            for s in range(SLOTS):
                split_high(0, s, s >= SPLITS)
            with act.Fori(0, BLOCKS - 1) as b:
                with act.Fori(1, GROUPS) as g:
                    for s in range(SLOTS):
                        split_high(b * GROUPS + g, s)
                for s in range(SLOTS):
                    split_high((b + 1) * GROUPS, s)
                    if s == 1:
                        take_sums((b + 1) * PIECES, slice(0, BLOCK))
            group = (BLOCKS - 1) * GROUPS
            with act.Fori(1, GROUPS // HALVES) as g:
                for s in range(SLOTS):
                    split_high(group + g, s)
            for s in range(SLOTS):
                split_high(group + GROUPS // HALVES, s)
                if s == 1:
                    take_sums(LAST - PIECES // HALVES, slice(0, BANK))
            for s in range(SLOTS - FINE_PIECES):
                split_high(group + GROUPS - 1, s)
            split_high_parts()
            take_sums(FIRST_FINE + len(parts), slice(BANK, BLOCK))

        @block.vector
        def _(dve):
            dve.wait_ge(u_loaded, DMA)
            nc.vector.tensor_scalar(dropped[:, :, :], dropped[:, :, :], P_DROP, 1.0 / (1.0 - P_DROP),
                                    ALU.is_ge, ALU.mult).then_inc(drop_scaled, 1)
            dve.wait_ge(drop_scaled, 1)
            dve.wait_ge(x_loaded, DMA)
            nc.vector.tensor_tensor(dropped[:, :, :], dropped[:, :, :], x_sb[:, :, :],
                                    ALU.mult).then_inc(x_dropped, 1)
            dve.wait_ge(weights_high, 1)
            nc.vector.tensor_tensor(weights[:, :, D:2 * D], dropped[:, :, :],
                                    weights[:, :, 0:D].bitcast(fp32),
                                    ALU.subtract).then_inc(weights_ready, 1)

            def split_low(g, s):
                dve.wait_ge(high_ready, g * SLOTS + s + 1)
                nc.vector.tensor_tensor(low[:, s % SPLITS, :], raw[:, s, :],
                                        high[:, s % SPLITS, :].bitcast(fp32),
                                        ALU.subtract).then_inc(low_ready, 1)

            def split_low_parts():
                for f, (piece, part) in enumerate(parts):
                    dve.wait_ge(high_ready, FIRST_FINE + f + 1)
                    nc.vector.tensor_tensor(low[:, piece % SPLITS, part], raw[:, piece % SLOTS, part],
                                            high[:, piece % SPLITS, part].bitcast(fp32),
                                            ALU.subtract).then_inc(low_ready, 1)

            def statistics(n, c, residual, used=None):
                dve.wait_ge(unit_turned, n + 1)
                if used is not None:
                    dve.wait_ge(normed_ready, used)
                nc.vector.tensor_tensor(rows[:, c, :], turned[:, c, :], residual,
                                        ALU.add).then_inc(rows_ready, 1)
                dve.wait_ge(rows_ready, n + 1)
                for i in range(c.start, c.stop):
                    last = nc.vector.bn_stats(stats[:, i, :], rows[:, i, :])
                last.then_inc(stats_ready, 1)
                dve.wait_ge(stats_ready, n + 1)
                nc.vector.tensor_tensor(mean[:, c], stats[:, c, 1], stats[:, c, 4], ALU.add)
                nc.vector.tensor_tensor(apart[:, c], stats[:, c, 1], stats[:, c, 4], ALU.subtract)
                nc.vector.tensor_tensor(squares[:, c], stats[:, c, 2], stats[:, c, 5],
                                        ALU.add).then_inc(parities_joined, 1)
                dve.wait_ge(parities_joined, n + 1)
                nc.vector.scalar_tensor_tensor(between[:, c], apart[:, c], 0.25, apart[:, c],
                                               ALU.mult, ALU.mult)
                nc.vector.tensor_scalar(squares[:, c], squares[:, c], 1.0 / D, EPS, ALU.mult, ALU.add)
                nc.vector.tensor_scalar(mean[:, c], mean[:, c], 0.5, None,
                                        ALU.mult).then_inc(moments_ready, 1)
                dve.wait_ge(moments_ready, n + 1)
                nc.vector.tensor_tensor(var_eps[:, c], squares[:, c], between[:, c],
                                        ALU.add).then_inc(var_ready, 1)

            def middle_block(b, used):
                with dve.Fori(1, GROUPS) as g:
                    for s in range(SLOTS):
                        split_low(b * GROUPS + g, s)
                for s in range(SLOTS):
                    split_low((b + 1) * GROUPS, s)
                    if s == SLOTS - 3:
                        residual = x_sb[:, bass.ds(b * CHUNKS_PER_BLOCK, CHUNKS_PER_BLOCK), :]
                        statistics(b, whole, residual, used)

            for s in range(SLOTS):
                split_low(0, s)
            middle_block(0, None)
            with dve.Fori(1, BLOCKS - 1) as b:
                middle_block(b, b)
            x_last = x_sb[:, CHUNKS - CHUNKS_PER_BLOCK:, :]
            group = (BLOCKS - 1) * GROUPS
            with dve.Fori(1, GROUPS // HALVES) as g:
                for s in range(SLOTS):
                    split_low(group + g, s)
            for s in range(SLOTS):
                split_low(group + GROUPS // HALVES, s)
                if s == SLOTS - 3:
                    statistics(BLOCKS - 1, half[0], x_last[:, half[0], :], BLOCKS - 1)
            for s in range(SLOTS - FINE_PIECES):
                split_low(group + GROUPS - 1, s)
            split_low_parts()
            c = half[1]
            statistics(BLOCKS, c, x_last[:, c, :])
            nc.vector.tensor_tensor(centred[:, c, :], rows[:, c, :], spread(mean, c),
                                    ALU.subtract).then_inc(last_centred, 1)
            dve.wait_ge(last_centred, 1)
            dve.wait_ge(rstd_ready, BLOCKS + 1)
            dve.wait_ge(out_stored, (BLOCKS - 1) * DMA)
            nc.vector.tensor_tensor(normed[:, c, :], centred[:, c, :], spread(rstd, c),
                                    ALU.mult).then_inc(last_normed, 1)

        @block.tensor
        def _(pe):
            def multiply_chunk(k, buffer, start, banks):
                for split in (high, low):
                    for n, bank in enumerate(banks):
                        last = nc.tensor.matmul(
                            acc[:, bank * BANK:(bank + 1) * BANK], weights[:, k, :],
                            split[:, buffer, start + n * BANK:start + (n + 1) * BANK],
                            start=(k == 0 and split is high), stop=(k == CHUNKS - 1 and split is low))
                return last

            def multiply(b, i):
                pe.wait_ge(low_ready, b * PIECES + i + 1)
                for j in range(K_PER_PIECE):
                    last = multiply_chunk(i * K_PER_PIECE + j, i % SPLITS, j * BLOCK, range(HALVES))
                last.then_inc(multiplied, 1)

            def multiply_half(h, i):
                piece = LAST - PIECES + h * PIECES // HALVES + i
                pe.wait_ge(low_ready, piece + 1)
                for j in range(K_PER_HALF_PIECE):
                    last = multiply_chunk(i * K_PER_HALF_PIECE + j, piece % SPLITS, j * BANK, (h,))
                last.then_inc(multiplied, 1)

            def multiply_parts():
                for f, (piece, part) in enumerate(parts):
                    pe.wait_ge(low_ready, FIRST_FINE + f + 1)
                    for start in range(part.start, part.stop, BANK):
                        k = CHUNKS - (LAST - piece) * K_PER_HALF_PIECE + start // BANK
                        last = multiply_chunk(k, piece % SPLITS, start, (HALVES - 1,))
                    last.then_inc(multiplied, 1)

            def turn(n, c):
                pe.wait_ge(sums_ready, n + 1)
                for i in range(c.start, c.stop):
                    last = nc.tensor.matmul(turned[:, i, :], sums[:, i * P:(i + 1) * P], join[:, :],
                                            start=True, stop=True)
                last.then_inc(unit_turned, 1)

            pe.wait_ge(weights_ready, 1)
            pe.wait_ge(join_ready, 1)
            with pe.Fori(0, BLOCKS - 1) as b:
                for i in range(PIECES):
                    multiply(b, i)
                turn(b, whole)
            for i in range(PIECES // HALVES):
                multiply_half(0, i)
            for i in range(2):
                multiply_half(1, i)
            turn(BLOCKS - 1, half[0])
            for i in range(2, PIECES // HALVES - FINE_PIECES):
                multiply_half(1, i)
            multiply_parts()
            turn(BLOCKS, half[1])


def kernel(x, adj, L0_gnn_u):
    import numpy as np
    import concourse.bacc as bacc
    from concourse.bass_utils import run_bass_kernel_spmd

    by_block = np.asarray(adj).reshape(P, BLOCKS, HALVES, CHUNKS_PER_HALF, P, CHUNKS)
    full = by_block[:, :-1].reshape(P, BLOCKS - 1, CHUNKS_PER_BLOCK, P, PIECES, K_PER_PIECE)
    full = full.transpose(1, 4, 3, 5, 2, 0).reshape(-1, P, PIECE)
    last = by_block[:, -1].reshape(P, HALVES, CHUNKS_PER_HALF, P, PIECES // HALVES, K_PER_HALF_PIECE)
    last = last.transpose(1, 4, 3, 5, 2, 0).reshape(-1, P, PIECE)
    arrays = {
        "x_dram": np.ascontiguousarray(x),
        "u_dram": np.ascontiguousarray(L0_gnn_u),
        "adj_dram": np.concatenate([full, last]),
    }
    nc = bacc.Bacc("TRN2", target_bir_lowering=False, num_devices=1)
    fp32 = mybir.dt.float32
    args = [nc.dram_tensor(name, a.shape, fp32, kind="ExternalInput").ap() for name, a in arrays.items()]
    out = nc.dram_tensor("out_dram", (N, D), fp32, kind="ExternalOutput").ap()
    dropout_matmul_layernorm(nc, *args, out)
    got = run_bass_kernel_spmd(nc, [arrays], core_ids=[0])
    return got.results[0]["out_dram"]
```
